# Optimizing a Trainium2 kernel written in Bass

```python
import numpy as np
import jax
import jax.numpy as jnp

def _softmax(x, axis=-1):
    return jax.nn.softmax(x, axis=axis)

def _gelu(x):
    return jax.nn.gelu(x, approximate=True)

def _silu(x):
    return jax.nn.silu(x)

def _sigmoid(x):
    return jax.nn.sigmoid(x)

def _layernorm(x, axis=-1, eps=1e-05):
    m = jnp.mean(x, axis=axis, keepdims=True)
    v = jnp.var(x, axis=axis, keepdims=True)
    return (x - m) / jnp.sqrt(v + eps)

def _scatter_add(tgt, idx, src, axis=0):
    return tgt.at[idx].add(src)

def _segment_sum(src, seg, n):
    return jax.ops.segment_sum(src, seg, n)
kernel_name = 'mk_gnn_preln_d2_gnn_r8_8c6726'

def setup_inputs(seed: int=0):
    np.random.seed(seed)
    _w = jnp.asarray

    def _rec_inputs():
        import jax
        import jax.numpy as jnp
        _gk = jax.random.key(seed)
        x = -0.0008691 + 1 * jax.random.normal(jax.random.fold_in(_gk, 1), (6250, 128), jnp.float32)
        _s = jax.random.randint(jax.random.fold_in(_gk, 2), (50000,), 0, 6250, jnp.int32)
        _d = jax.random.randint(jax.random.fold_in(_gk, 3), (50000,), 0, 6250, jnp.int32)
        _loop = jnp.arange(6250, dtype=jnp.int32)
        src = jnp.concatenate([_s, _d, _loop])
        dst = jnp.concatenate([_d, _s, _loop])
        _o = jnp.argsort(dst, stable=True)
        src = src[_o]
        dst = dst[_o]
        return (x, src, dst)
    x, src, dst = _rec_inputs()

    def _L0_gnn_setup():
        import jax, jax.numpy as jnp
        import numpy as np
        N_NODES = 1250
        N_EDGES = 80000
        IN_DIM = 128
        OUT_DIM = 128
        key = jax.random.key(seed)
        k1, k2, k3 = jax.random.split(key, 3)
        x = jax.random.normal(k1, (N_NODES, IN_DIM), dtype=jnp.float32)
        edge_index = jax.random.randint(k2, (2, N_EDGES), 0, N_NODES, dtype=jnp.int64)
        W = jax.random.normal(k3, (IN_DIM, OUT_DIM), dtype=jnp.float32) * (1.0 / np.sqrt(IN_DIM))
        b = jnp.zeros((OUT_DIM,), dtype=jnp.float32)
        return {'x': x, 'edge_index': edge_index, 'W': W, 'b': b}
    _L0_gnn_all = _L0_gnn_setup()
    _L0_gnn_in = {k: v for k, v in _L0_gnn_all.items() if k in ('W', 'b')}
    del _L0_gnn_all

    def _L1_gnn_setup():
        import jax, jax.numpy as jnp
        import numpy as np
        D_MODEL = 128
        N_HEADS = 8
        HEAD_DIM = D_MODEL // N_HEADS
        N_NODES = 6250
        N_EDGES = 80000
        key = jax.random.key(seed)
        ks = jax.random.split(key, 10)
        sd = 1.0 / np.sqrt(D_MODEL)
        return {'node_embeds': jax.random.normal(ks[0], (N_NODES, D_MODEL), dtype=jnp.float32), 'edge_index': jax.random.randint(ks[1], (2, N_EDGES), 0, N_NODES, dtype=jnp.int64), 'Wq': jax.random.uniform(ks[2], (D_MODEL, D_MODEL), jnp.float32, -sd, sd), 'bq': jax.random.uniform(ks[3], (D_MODEL,), jnp.float32, -sd, sd), 'Wk': jax.random.uniform(ks[4], (D_MODEL, D_MODEL), jnp.float32, -sd, sd), 'bk': jax.random.uniform(ks[5], (D_MODEL,), jnp.float32, -sd, sd), 'Wv': jax.random.uniform(ks[6], (D_MODEL, D_MODEL), jnp.float32, -sd, sd), 'bv': jax.random.uniform(ks[7], (D_MODEL,), jnp.float32, -sd, sd), 'gamma': jnp.ones((D_MODEL,), jnp.float32), 'beta': jnp.zeros((D_MODEL,), jnp.float32)}
    _L1_gnn_all = _L1_gnn_setup()
    _L1_gnn_in = {k: v for k, v in _L1_gnn_all.items() if k in ('Wq', 'bq', 'Wk', 'bk', 'Wv', 'bv', 'gamma', 'beta')}
    del _L1_gnn_all
    return {'x': x, 'src': src, 'dst': dst, 'L0_gnn_W': _L0_gnn_in['W'], 'L0_gnn_b': _L0_gnn_in['b'], 'L1_gnn_Wq': _L1_gnn_in['Wq'], 'L1_gnn_bq': _L1_gnn_in['bq'], 'L1_gnn_Wk': _L1_gnn_in['Wk'], 'L1_gnn_bk': _L1_gnn_in['bk'], 'L1_gnn_Wv': _L1_gnn_in['Wv'], 'L1_gnn_bv': _L1_gnn_in['bv'], 'L1_gnn_gamma': _L1_gnn_in['gamma'], 'L1_gnn_beta': _L1_gnn_in['beta']}

def reference(x, src, dst, L0_gnn_W, L0_gnn_b, L1_gnn_Wq, L1_gnn_bq, L1_gnn_Wk, L1_gnn_bk, L1_gnn_Wv, L1_gnn_bv, L1_gnn_gamma, L1_gnn_beta):
    import jax
    import jax.numpy as jnp

    def _L0_gnn_ref(x, edge_index, W, b):
        import jax, jax.numpy as jnp
        import numpy as np
        N_NODES = 1250
        N_EDGES = 80000
        IN_DIM = 128
        OUT_DIM = 128
        n = x.shape[0]
        loop = jnp.arange(n, dtype=edge_index.dtype)
        src = jnp.concatenate([edge_index[0], loop])
        dst = jnp.concatenate([edge_index[1], loop])
        xw = x @ W
        ones = jnp.ones(dst.shape, dtype=x.dtype)
        deg = jax.ops.segment_sum(ones, dst, num_segments=n)
        dinv = jnp.where(deg > 0, jax.lax.rsqrt(deg), 0.0)
        norm = dinv[src] * dinv[dst]
        msg = xw[src] * norm[:, None]
        out = jax.ops.segment_sum(msg, dst, num_segments=n) + b
        return jax.nn.relu(out)

    def _L1_gnn_ref(node_embeds, edge_index, Wq, bq, Wk, bk, Wv, bv, gamma, beta):
        import jax, jax.numpy as jnp
        import numpy as np
        D_MODEL = 128
        N_HEADS = 8
        HEAD_DIM = D_MODEL // N_HEADS
        N_NODES = 6250
        N_EDGES = 80000
        num_nodes = node_embeds.shape[0]
        rows, cols = (edge_index[0], edge_index[1])
        src = node_embeds[rows]
        tgt = node_embeds[cols]
        q = (src @ Wq.T + bq).reshape(-1, N_HEADS, HEAD_DIM)
        k = (tgt @ Wk.T + bk).reshape(-1, N_HEADS, HEAD_DIM)
        v = (tgt @ Wv.T + bv).reshape(-1, N_HEADS, HEAD_DIM)
        att = jnp.einsum('ehd,ehd->eh', q, k) / jnp.sqrt(jnp.float32(HEAD_DIM))
        exp_att = jnp.exp(jnp.clip(att, -10.0, 10.0))
        att_sum = jax.ops.segment_sum(exp_att, rows, num_segments=num_nodes)
        att_norm = exp_att / (att_sum[rows] + 1e-08)
        weighted_v = (att_norm[..., None] * v).reshape(-1, D_MODEL)
        out = jax.ops.segment_sum(weighted_v, rows, num_segments=num_nodes)
        out = out + node_embeds
        mu = jnp.mean(out, axis=-1, keepdims=True)
        var = jnp.mean(jnp.square(out - mu), axis=-1, keepdims=True)
        out = (out - mu) * jax.lax.rsqrt(var + 1e-06) * gamma + beta
        return out
    edge_index = jnp.stack([src, dst])
    h = jnp.maximum(_layernorm(x, axis=-1), 0.0)
    x = x + _L0_gnn_ref(h, edge_index, L0_gnn_W, L0_gnn_b)
    h = jnp.maximum(_layernorm(x, axis=-1), 0.0)
    x = x + _L1_gnn_ref(h, edge_index, L1_gnn_Wq, L1_gnn_bq, L1_gnn_Wk, L1_gnn_bk, L1_gnn_Wv, L1_gnn_bv, L1_gnn_gamma, L1_gnn_beta)
    return x

_drawn_inputs = setup_inputs


def setup_inputs(seed=0):
    import zlib

    import numpy as np

    out = dict(_drawn_inputs(seed))
    spreads = {'L0_gnn_b': (0.0, 0.1), 'L1_gnn_gamma': (1.0, 0.2), 'L1_gnn_beta': (0.0, 0.1)}
    factors = {'L1_gnn_Wq': 5.994, 'L1_gnn_bq': 8.0, 'L1_gnn_Wk': 5.966, 'L1_gnn_bk': 8.0}
    for name, (base, spread) in spreads.items():
        noise = np.random.default_rng([zlib.crc32(name.encode()), seed]).standard_normal(out[name].shape)
        drawn = base * np.exp(spread * noise) if base else spread * noise
        out[name] = jnp.asarray(drawn.astype(out[name].dtype))
    for name, factor in factors.items():
        out[name] = (out[name] * factor).astype(out[name].dtype)
    return out
```

```python
import concourse.bass as bass
from concourse import mybir
from contextlib import ExitStack

F32, F16, BF16 = mybir.dt.float32, mybir.dt.float16, mybir.dt.bfloat16
I32, U16 = mybir.dt.int32, mybir.dt.uint16
ALU = mybir.AluOpType
ACT = mybir.ActivationFunctionType
AX = mybir.AxisListType
ds = bass.ds

P = 128
D = 128
HEADS, HD = 8, 16
NODES, EDGES = 6250, 106250
NB = -(-NODES // P)
NT = NB + NB % 2
GROUP = 16
HALF = GROUP // 2
ET = -(-EDGES // (P * GROUP)) * GROUP
LAST_TILE, LAST_FILL = EDGES // P, EDGES % P
ST = -(-(EDGES // P + NB) // GROUP) * GROUP
MSG = D + HEADS
NOWHERE = float(P * (ST + P))
EPS_H, EPS_OUT, EPS_SUM = 1e-5, 1e-6, 1e-8


def build(nc, x_in, src_in, dst_in, dst_rows_in, w0_in, b0_in, wqkv_in, bqkv_in, gamma_in, beta_in,
          y_tab, kv_tab, out):
    ctx = ExitStack()

    def sb(name, shape, dt=F32):
        return ctx.enter_context(nc.sbuf_tensor(name, shape, dt))

    def sem(name):
        return ctx.enter_context(nc.semaphore(name))

    with ctx:
        x = sb("x", [P, NT, D])
        h = sb("h", [P, NT, D])
        acc = sb("acc", [P, NT, MSG])
        dinv = sb("dinv", [P, NT])
        stats = sb("stats", [P, NT, 6])
        mean = sb("mean", [P, NT])
        skew = sb("skew", [P, NT])
        rstd = sb("rstd", [P, NT])
        nbias = sb("nbias", [P, NT])
        src_c = sb("src_c", [P, ET], I32)
        dst_f = sb("dst_f", [P, ET])
        dst_rel = sb("dst_rel", [P, ET + 2])
        lo_c = sb("lo_c", [P, ET])
        hi_c = sb("hi_c", [P, ET])
        val1 = sb("val1", [P, ET])
        val2 = sb("val2", [P, ET])
        lo_tab = sb("lo_tab", [1, P * 7], I32)
        more_tab = sb("more_tab", [1, P * 7], I32)
        hi_tab = sb("hi_tab", [1, P * 7], I32)
        past_tab = sb("past_tab", [1, P * 7], I32)
        step_tab = sb("step_tab", [1, P * 7], I32)
        bucket_tab = sb("bucket_tab", [1, P * 7], I32)
        iota = sb("iota", [P, P * 7])
        iota_h = sb("iota_h", [P, ST], F16)
        lane = sb("lane", [P, 1])
        ident = sb("ident", [P, P])
        ones = sb("ones", [P, P])
        base = sb("base", [P, NT])
        w0 = sb("w0", [D, D])
        wqkv = sb("wqkv", [D, 3 * D])
        b0 = sb("b0", [1, D])
        bqkv = sb("bqkv", [1, 3 * D])
        gamma = sb("gamma", [P, D])
        beta = sb("beta", [P, D])
        src_s = sb("src_s", [P, ST + GROUP])
        dst_s = sb("dst_s", [P, ST], I32)

        def moments(then, eps):
            then(nc.vector.tensor_tensor(mean[:, :], stats[:, :, 1], stats[:, :, 4], ALU.add))
            then(nc.vector.tensor_scalar(mean[:, :], mean[:, :], 0.5, None, ALU.mult))
            then(nc.vector.tensor_tensor(skew[:, :], stats[:, :, 1], mean[:, :], ALU.subtract))
            then(nc.vector.tensor_tensor(skew[:, :], skew[:, :], skew[:, :], ALU.mult))
            then(nc.vector.tensor_tensor(rstd[:, :], stats[:, :, 2], stats[:, :, 5], ALU.add))
            then(nc.vector.tensor_scalar(rstd[:, :], rstd[:, :], 1.0 / D, eps, ALU.mult, ALU.add))
            return nc.vector.tensor_tensor(rstd[:, :], rstd[:, :], skew[:, :], ALU.add)

        with ExitStack() as c1, nc.Block() as block:
            def sb1(name, shape, dt=F32):
                return c1.enter_context(nc.sbuf_tensor(name, shape, dt))

            def ps1(name, shape):
                return c1.enter_context(nc.psum_tensor(name, shape, F32))

            iota_i = sb1("iota_i", [P, P * 7], I32)
            lane_i = sb1("lane_i", [P, 1], I32)
            bad = sb1("bad", [P, 1])
            lower = sb1("lower", [P, P])
            dst_c = sb1("dst_c", [P, ET], I32)
            dst_rows = sb1("dst_rows", [P, 7, P], I32)
            dst_rows_f = sb1("dst_rows_f", [P, 7, P])
            ends_f = sb1("ends_f", [P, 2, 7])
            ends_i = sb1("ends_i", [P, 2, 7], I32)
            row_f = sb1("row_f", [1, 3, P * 7])
            zrow = sb1("zrow", [1, P * 7])
            tmp_i = sb1("tmp_i", [P, ET], I32)
            tmp_f = sb1("tmp_f", [P, ET])
            dlo = sb1("dlo", [P, ET], F16)
            dhi = sb1("dhi", [P, ET], F16)
            ohlo = sb1("ohlo", [P, 2, HALF, P], BF16)
            ohhi = sb1("ohhi", [P, 2, HALF, NT], BF16)
            deg = sb1("deg", [P, NT])
            sbk = sb1("sbk", [P, ET], F16)
            ohb = sb1("ohb", [P, ET], F16)
            zeros_h = sb1("zeros_h", [P, ET], F16)
            run = sb1("run", [P, ET])
            pos = sb1("pos", [P, ET])
            count = sb1("count", [P, NT])
            first = sb1("first", [P, NT])
            tiles_i = sb1("tiles_i", [P, NT], I32)
            tiles = sb1("tiles", [P, NT])
            tend = sb1("tend", [P, NT])
            junk = sb1("junk", [P, NT])
            bk = sb1("bk", [P, 7])
            run_i = run[:, :].bitcast(I32)
            ps_row = ps1("ps_row", [1, 1024])
            ps_row2 = ps1("ps_row2", [1, 1024])
            ps_lo = ps1("ps_lo", [P, 1024])
            ps_deg = ps1("ps_deg", [P, 512])
            ps_cnt = ps1("ps_cnt", [P, 512])

            in_x, in_e, in_w = sem("in_x"), sem("in_e"), sem("in_w")
            iota_ready = sem("iota_ready")
            dve1 = sem("dve1")
            ends_ready, lo_row_ready = sem("ends_ready"), sem("lo_row_ready")
            rows_done, lo_bc_done = sem("rows_done"), sem("lo_bc_done")
            hot_ready, hot_used, deg_done = sem("hot_ready"), sem("hot_used"), sem("deg_done")
            var_ready, std_done, norm_ready, h_done = sem("var_ready"), sem("std_done"), sem("norm_ready"), sem("h_done")
            deg_ready, sdeg_done, y_ready, y_stored = sem("deg_ready"), sem("sdeg_done"), sem("y_ready"), sem("y_stored")
            acc_set = sem("acc_set")
            count_ready, count_done, bk_ready, bk_row_done = sem("count_ready"), sem("count_done"), sem("bk_ready"), sem("bk_row_done")

            @block.sync
            def _(sp):
                sp.dma_start(dst_rows[:, :, :], dst_rows_in).then_inc(in_e, 16)
                sp.dma_start(dst_c[:, :], dst_in).then_inc(in_e, 16)
                sp.dma_start(src_c[:, :], src_in).then_inc(in_e, 16)
                sp.dma_start(x[:, :, :], x_in).then_inc(in_x, 16)
                sp.dma_start(w0[:, :], w0_in).then_inc(in_w, 16)
                sp.dma_start(wqkv[:, :], wqkv_in).then_inc(in_w, 16)
                sp.dma_start(b0[:, :], b0_in).then_inc(in_w, 16)
                sp.dma_start(bqkv[:, :], bqkv_in).then_inc(in_w, 16)
                sp.dma_start(gamma[:, :], gamma_in).then_inc(in_w, 16)
                sp.dma_start(beta[:, :], beta_in).then_inc(in_w, 16)
                sp.wait_ge(in_w, 16 * 6)
                sp.wait_ge(y_ready, 1)
                sp.dma_start(y_tab.rearrange("(j p) d -> p j d", p=P), h[:, :, :]).then_inc(y_stored, 16)
                sp.wait_ge(y_stored, 16)

            @block.gpsimd
            def _(pool):
                nc.gpsimd.iota(iota_i[:, :], [[1, P * 7]], base=0, channel_multiplier=0).then_inc(iota_ready, 1)
                nc.gpsimd.iota(lane_i[:, :], [[1, 1]], base=0, channel_multiplier=1).then_inc(iota_ready, 1)

            @block.vector
            def _(v):
                steps = [0]

                def then(ins):
                    steps[0] += 1
                    ins.then_inc(dve1, 1)
                    v.wait_ge(dve1, steps[0])

                v.wait_ge(iota_ready, 2)
                then(nc.vector.tensor_copy(lane[:, :], lane_i[:, :]))
                then(nc.vector.tensor_copy(iota[:, :], iota_i[:, :]))
                then(nc.vector.tensor_copy(iota_h[:, :], iota[:, 0:ST]))
                then(nc.vector.tensor_scalar(ident[:, :], iota[:, 0:P], lane[:, :], None, ALU.is_equal))
                then(nc.vector.tensor_scalar(lower[:, :], iota[:, 0:P], lane[:, :], None, ALU.is_gt))
                then(nc.vector.memset(ones[:, :], 1.0))
                then(nc.vector.tensor_scalar(base[:, :], iota[:, 0:NT], float(P), None, ALU.mult))
                then(nc.vector.memset(zrow[:, :], 0.0))
                then(nc.vector.memset(zeros_h[:, :], 0.0))
                then(nc.vector.tensor_scalar(bad[:, :], lane[:, :], float(LAST_FILL), 2048.0, ALU.is_ge, ALU.mult))

                v.wait_ge(in_e, 48)
                then(nc.vector.tensor_copy(dst_rows_f[:, :, :], dst_rows[:, :, :]))
                then(nc.vector.tensor_reduce(ends_f[:, 0, :], dst_rows_f[:, :, :], AX.X, ALU.min))
                then(nc.vector.tensor_reduce(ends_f[:, 1, :], dst_rows_f[:, :, :], AX.X, ALU.max))
                then(nc.vector.tensor_copy(ends_i[:, :, :], ends_f[:, :, :]))
                then(nc.vector.tensor_scalar(ends_i[:, :, :], ends_i[:, :, :], 7, None, ALU.arith_shift_right))
                then(nc.vector.tensor_copy(ends_f[:, :, :], ends_i[:, :, :]))
                nc.vector.tensor_tensor(ends_f[:, 1, :], ends_f[:, 1, :], ends_f[:, 0, :],
                                        ALU.subtract).then_inc(ends_ready, 1)

                then(nc.vector.tensor_copy(dst_f[:, :], dst_c[:, :]))
                then(nc.vector.tensor_scalar(tmp_i[:, :], dst_c[:, :], 7, None, ALU.arith_shift_right))
                then(nc.vector.tensor_copy(dhi[:, :], tmp_i[:, :]))
                then(nc.vector.tensor_scalar(tmp_i[:, :], dst_c[:, :], P - 1, None, ALU.bitwise_and))
                then(nc.vector.tensor_copy(dlo[:, :], tmp_i[:, :]))
                then(nc.vector.tensor_scalar(dlo[:, LAST_TILE:LAST_TILE + 1], dlo[:, LAST_TILE:LAST_TILE + 1],
                                             bad[:, :], None, ALU.add))
                then(nc.vector.memset(dlo[:, LAST_TILE + 1:ET], 2048.0))

                with v.Fori(0, ET // GROUP) as i:
                    for s in range(2):
                        v.wait_ge(hot_used, i * 2 + s + 1)
                        cols = ds(i * GROUP + s * HALF, HALF)
                        nc.vector.tensor_tensor(ohhi[:, s, :, :],
                                                iota_h[:, 0:NT].unsqueeze(1).to_broadcast([P, HALF, NT]),
                                                dhi[:, cols].unsqueeze(2).to_broadcast([P, HALF, NT]), ALU.is_equal)
                        nc.vector.tensor_tensor(ohlo[:, s, :, :],
                                                iota_h[:, 0:P].unsqueeze(1).to_broadcast([P, HALF, P]),
                                                dlo[:, cols].unsqueeze(2).to_broadcast([P, HALF, P]),
                                                ALU.is_equal).then_inc(hot_ready, 1)

                v.wait_ge(in_x, 16)
                with v.Fori(0, NT) as j:
                    nc.vector.bn_stats(stats[:, ds(j, 1), :], x[:, ds(j, 1), :]).then_inc(dve1, 1)
                steps[0] += NT
                v.wait_ge(dve1, steps[0])
                moments(then, EPS_H).then_inc(var_ready, 1)
                v.wait_ge(std_done, 1)
                then(nc.vector.reciprocal(rstd[:, :], rstd[:, :]))
                nc.vector.scalar_tensor_tensor(out=nbias[:, :], in0=mean[:, :], scalar=-1.0, in1=rstd[:, :],
                                               op0=ALU.mult, op1=ALU.mult).then_inc(norm_ready, 1)

                v.wait_ge(deg_done, 1)
                nc.vector.tensor_scalar(deg[:, :], ps_deg[:, 0:NT], 1.0, None, ALU.add).then_inc(deg_ready, 1)
                v.wait_ge(sdeg_done, 1)
                then(nc.vector.reciprocal(dinv[:, :], deg[:, :]))
                v.wait_ge(h_done, NT)
                nc.vector.tensor_tensor(h[:, :, :], h[:, :, :],
                                        dinv[:, :].unsqueeze(2).to_broadcast([P, NT, D]), ALU.mult).then_inc(y_ready, 1)
                v.wait_ge(y_ready, 1)
                nc.vector.tensor_copy(acc[:, :, 0:D], h[:, :, :]).then_inc(acc_set, 1)

                v.wait_ge(rows_done, 1)
                then(nc.vector.tensor_copy(row_f[:, 0, :], ps_row[:, 0:P * 7]))
                nc.vector.tensor_copy(row_f[:, 1, :], ps_row2[:, 0:P * 7]).then_inc(lo_row_ready, 1)
                v.wait_ge(lo_row_ready, 1)
                then(nc.vector.tensor_copy(lo_tab[:, :], row_f[:, 0, :]))
                then(nc.vector.tensor_copy(more_tab[:, :], row_f[:, 1, :]))
                then(nc.vector.tensor_tensor_scan(row_f[:, 2, :], row_f[:, 1, :], zrow[:, :], 0.0, ALU.add, ALU.add))
                then(nc.vector.tensor_tensor(row_f[:, 2, :], row_f[:, 2, :], row_f[:, 1, :], ALU.subtract))
                then(nc.vector.tensor_tensor(hi_tab[:, :], lo_tab[:, :], more_tab[:, :], ALU.add))
                then(nc.vector.tensor_copy(past_tab[:, :], row_f[:, 2, :]))
                then(nc.vector.scalar_tensor_tensor(out=step_tab[:, :], in0=row_f[:, 2, :], scalar=float(NB),
                                                    in1=row_f[:, 0, :], op0=ALU.add, op1=ALU.subtract))
                v.wait_ge(lo_bc_done, 1)
                then(nc.vector.scalar_tensor_tensor(out=dst_rel[:, 0:ET], in0=ps_lo[:, 0:ET], scalar=-float(P),
                                                    in1=dst_f[:, :], op0=ALU.mult, op1=ALU.add))
                then(nc.vector.scalar_tensor_tensor(out=dst_rel[:, LAST_TILE:LAST_TILE + 1], in0=bad[:, :],
                                                    scalar=16.0, in1=dst_rel[:, LAST_TILE:LAST_TILE + 1],
                                                    op0=ALU.mult, op1=ALU.add))
                then(nc.vector.memset(dst_rel[:, LAST_TILE + 1:ET + 2], 32768.0))
                then(nc.vector.scalar_tensor_tensor(out=dst_f[:, LAST_TILE:LAST_TILE + 1], in0=bad[:, :],
                                                    scalar=16.0, in1=dst_f[:, LAST_TILE:LAST_TILE + 1],
                                                    op0=ALU.mult, op1=ALU.add))
                then(nc.vector.memset(dst_f[:, LAST_TILE + 1:ET], 32768.0))

                then(nc.vector.tensor_scalar(tmp_i[:, :], src_c[:, :], P - 1, None, ALU.bitwise_and))
                then(nc.vector.tensor_copy(val1[:, :], tmp_i[:, :]))
                then(nc.vector.tensor_scalar(tmp_i[:, :], dst_c[:, :], 11, None, ALU.arith_shift_right))
                then(nc.vector.tensor_copy(tmp_f[:, :], tmp_i[:, :]))
                then(nc.vector.tensor_scalar(tmp_f[:, :], tmp_f[:, :], 256.0, 1.0, ALU.mult, ALU.add))
                then(nc.vector.tensor_tensor(val1[:, :], val1[:, :], tmp_f[:, :], ALU.add))
                then(nc.vector.tensor_scalar(tmp_i[:, :], dst_c[:, :], 2047, None, ALU.bitwise_and))
                then(nc.vector.tensor_copy(val2[:, :], tmp_i[:, :]))

                then(nc.vector.tensor_scalar(tmp_i[:, :], src_c[:, :], 7, None, ALU.arith_shift_right))
                then(nc.vector.tensor_copy(sbk[:, :], tmp_i[:, :]))
                then(nc.vector.tensor_scalar(sbk[:, LAST_TILE:LAST_TILE + 1], sbk[:, LAST_TILE:LAST_TILE + 1],
                                             bad[:, :], None, ALU.add))
                then(nc.vector.memset(sbk[:, LAST_TILE + 1:ET], 2048.0))
                with v.Fori(0, NB) as b:
                    nc.vector.tensor_scalar(ohb[:, :], sbk[:, :], iota[:, ds(b, 1)], None, ALU.is_equal, ALU.add,
                                            accum_out=count[:, ds(b, 1)]).then_inc(dve1, 1)
                    v.wait_ge(dve1, steps[0] + b + 1)
                steps[0] += NB
                nc.vector.memset(pos[:, :], 0.0).then_inc(count_ready, 1)
                v.wait_ge(count_done, 1)
                then(nc.vector.tensor_scalar(tiles_i[:, 0:NB], ps_cnt[:, 0:NB], float(P - 1), None, ALU.add))
                then(nc.vector.tensor_scalar(tiles_i[:, 0:NB], tiles_i[:, 0:NB], 7, None, ALU.arith_shift_right))
                then(nc.vector.tensor_copy(tiles[:, 0:NB], tiles_i[:, 0:NB]))
                then(nc.vector.tensor_tensor_scan(tend[:, 0:NB], tiles[:, 0:NB], zeros_h[:, 0:NB], 0.0, ALU.add, ALU.add))
                then(nc.vector.tensor_tensor(tiles[:, 0:NB], tend[:, 0:NB], tiles[:, 0:NB], ALU.subtract))
                then(nc.vector.tensor_scalar(tiles[:, 0:NB], tiles[:, 0:NB], float(P), -1.0, ALU.mult, ALU.add))
                then(nc.vector.tensor_tensor(first[:, 0:NB], tiles[:, 0:NB], ps_cnt[:, 64:64 + NB], ALU.add))
                for g in range(7):
                    then(nc.vector.tensor_scalar(junk[:, 0:1], lane[:, :], float(P * g), None, ALU.add))
                    then(nc.vector.tensor_scalar(junk[:, 1:1 + NB], tend[:, 0:NB], junk[:, 0:1], None, ALU.is_le, ALU.add,
                                                 accum_out=bk[:, g:g + 1]))
                nc.vector.tensor_scalar(bk[:, :], bk[:, :], float(NB - 1), None, ALU.min).then_inc(bk_ready, 1)
                with v.Fori(0, NB) as b:
                    nc.vector.tensor_scalar(ohb[:, :], sbk[:, :], iota[:, ds(b, 1)], None, ALU.is_equal).then_inc(dve1, 1)
                    v.wait_ge(dve1, steps[0] + 4 * b + 1)
                    nc.vector.tensor_tensor_scan(run[:, :], ohb[:, :], zeros_h[:, :], first[:, ds(b, 1)],
                                                 ALU.add, ALU.add).then_inc(dve1, 1)
                    v.wait_ge(dve1, steps[0] + 4 * b + 2)
                    nc.vector.tensor_tensor(run[:, :], run[:, :], ohb[:, :], ALU.mult).then_inc(dve1, 1)
                    v.wait_ge(dve1, steps[0] + 4 * b + 3)
                    nc.vector.tensor_tensor(pos[:, :], pos[:, :], run[:, :], ALU.add).then_inc(dve1, 1)
                    v.wait_ge(dve1, steps[0] + 4 * b + 4)
                steps[0] += 4 * NB
                then(nc.vector.scalar_tensor_tensor(out=pos[:, LAST_TILE:LAST_TILE + 1], in0=bad[:, :], scalar=64.0,
                                                    in1=pos[:, LAST_TILE:LAST_TILE + 1], op0=ALU.mult, op1=ALU.add))
                then(nc.vector.memset(pos[:, LAST_TILE + 1:ET], NOWHERE))
                then(nc.vector.tensor_copy(tmp_i[:, :], pos[:, :]))
                then(nc.vector.tensor_scalar(run_i, tmp_i[:, :], P - 1, None, ALU.bitwise_and))
                then(nc.vector.tensor_copy(lo_c[:, :], run_i))
                then(nc.vector.tensor_scalar(tmp_i[:, :], tmp_i[:, :], 7, None, ALU.arith_shift_right))
                then(nc.vector.tensor_copy(hi_c[:, :], tmp_i[:, :]))
                v.wait_ge(bk_row_done, 1)
                then(nc.vector.tensor_copy(bucket_tab[:, :], ps_row[:, 0:P * 7]))

            @block.scalar
            def _(act):
                act.wait_ge(var_ready, 1)
                nc.scalar.activation(rstd[:, :], rstd[:, :], ACT.Sqrt).then_inc(std_done, 1)
                act.wait_ge(norm_ready, 1)
                with act.Fori(0, NT) as j:
                    nc.scalar.activation(h[:, ds(j, 1), :], x[:, ds(j, 1), :], ACT.Relu, bias=nbias[:, ds(j, 1)],
                                         scale=rstd[:, ds(j, 1)]).then_inc(h_done, 1)
                act.wait_ge(deg_ready, 1)
                nc.scalar.activation(deg[:, :], deg[:, :], ACT.Sqrt).then_inc(sdeg_done, 1)

            @block.tensor
            def _(pe):
                pe.sem_inc(hot_used, 2)

                def to_row(row, col, done):
                    for g in range(7):
                        last = nc.tensor.matmul(row[:, g * P:(g + 1) * P], col[:, g:g + 1], ident[:, :], start=True, stop=True)
                    last.then_inc(done, 1)

                pe.wait_ge(ends_ready, 1)
                for g in range(7):
                    nc.tensor.matmul(ps_row[:, g * P:(g + 1) * P], ends_f[:, 0, g:g + 1], ident[:, :], start=True, stop=True)
                to_row(ps_row2, ends_f[:, 1, :], rows_done)
                def degrees(i, s, start, stop):
                    pe.wait_ge(hot_ready, i * 2 + s + 1)
                    for k in range(HALF):
                        last = nc.tensor.matmul(ps_deg[:, 0:NT], ohlo[:, s, k, :], ohhi[:, s, k, :],
                                                start=start and k == 0, stop=stop and k == HALF - 1)
                    return last

                degrees(0, 0, True, False).then_inc(hot_used, 1)
                degrees(0, 1, False, False).then_inc(hot_used, 1)
                with pe.Fori(1, ET // GROUP - 1) as i:
                    for s in range(2):
                        degrees(i, s, False, False).then_inc(hot_used, 1)
                degrees(ET // GROUP - 1, 0, False, False).then_inc(hot_used, 1)
                degrees(ET // GROUP - 1, 1, False, True).then_inc(deg_done, 1)
                pe.wait_ge(lo_row_ready, 1)
                for c in range(0, ET, 512):
                    w = min(512, ET - c)
                    last = nc.tensor.matmul(ps_lo[:, c:c + w], ones[0:1, :], row_f[0:1, 0, c:c + w], start=True, stop=True)
                last.then_inc(lo_bc_done, 1)
                pe.wait_ge(count_ready, 1)
                nc.tensor.matmul(ps_cnt[:, 0:NB], ones[:, :], count[:, 0:NB], start=True, stop=True)
                nc.tensor.matmul(ps_cnt[:, 64:64 + NB], lower[:, :], count[:, 0:NB], start=True, stop=True).then_inc(count_done, 1)
                pe.wait_ge(bk_ready, 1)
                to_row(ps_row, bk, bk_row_done)

        with ExitStack() as c2, nc.Block() as block:
            def sb2(name, shape, dt=F32):
                return c2.enter_context(nc.sbuf_tensor(name, shape, dt))

            def ps2(name, shape):
                return c2.enter_context(nc.psum_tensor(name, shape, F32))

            idx = sb2("idx0", [P, 2, HALF], I32)
            rows = sb2("rows0", [P, GROUP, D])
            hot = sb2("hot0", [P, 4, P])
            more_rel = sb2("more_rel", [P, 1])
            more_hot = sb2("more_hot", [P, P])
            sort_lo = sb2("sort_lo", [P, 2, 2, P], F16)
            sort_hi = sb2("sort_hi", [P, 2, ST], F16)
            zero_h = sb2("zero_h", [P, 512], F16)
            v1_i = sb2("v1_i", [P, ST], I32)
            v1_t = sb2("v1_t", [P, ST], I32)
            v1_f = sb2("v1_f", [P, ST])
            ps_sum = [ps2(f"ps_sum{k}", [P, 512]) for k in range(2)]
            ps_more = ps2("ps_more", [P, 512])
            ps_sort = [ps2(f"ps_sort{k}", [P, 1024]) for k in range(2)]

            idx_set, rows_in = sem("idx_set0"), [sem(f"rows_in0_{k}") for k in range(GROUP)]
            hot_ready, sum_done, acc_done = sem("hot_ready0"), sem("sum_done0"), sem("acc_done0")
            more_rel_set, more_hot_ready, more_sum_done, more_acc_done = (
                sem("more_rel_set"), sem("more_hot_ready"), sem("more_sum_done"), sem("more_acc_done"))
            sort_ready, sort_used, sort_done, dec = sem("sort_ready"), sem("sort_used"), sem("sort_done"), sem("decoded")
            zero_set = sem("zero_set")

            @block.gpsimd
            def _(pool):
                with pool.Fori(0, ET // GROUP) as i:
                    for s in range(2):
                        pool.wait_ge(sum_done, i * GROUP + (s + 1) * HALF)
                        nc.gpsimd.tensor_copy(idx[:, s, :], src_c[:, ds(i * GROUP + s * HALF, HALF)]).then_inc(idx_set, 1)
                        pool.wait_ge(idx_set, i * 2 + s + 1)
                        pool.nop(nofuse=True)
                        for k in range(s * HALF, (s + 1) * HALF):
                            pool.indirect_dma_start(
                                out=rows[:, k, :], out_offset=None, in_=y_tab,
                                in_offset=bass.IndirectOffsetOnAxis(ap=idx[:, s, k - s * HALF:k - s * HALF + 1], axis=0),
                            ).then_inc(rows_in[k], 16)

            @block.vector
            def _(v):
                nc.vector.memset(zero_h[:, :], 0.0).then_inc(zero_set, 1)

                def one_hot(t, slot):
                    v.wait_ge(sum_done, GROUP - 4 + t + 1)
                    nc.vector.tensor_scalar(hot[:, slot, :], iota[:, 0:P], dst_rel[:, ds(t, 1)], None,
                                            ALU.is_equal).then_inc(hot_ready, 1)

                v.sem_inc(acc_done, 2)
                v.sem_inc(more_rel_set, NB)
                v.sem_inc(more_hot_ready, NB)
                v.sem_inc(more_acc_done, NB + 1)
                one_hot(0, 0)
                one_hot(1, 1)
                with v.Fori(0, ET // GROUP) as i:
                    for k in range(GROUP):
                        t = i * GROUP + k
                        one_hot(t + 2, (k + 2) % 4)
                        v.wait_ge(sort_used, t + 1)
                        nc.vector.tensor_scalar(sort_lo[:, k % 2, 0, :], iota_h[:, 0:P], lo_c[:, ds(t, 1)],
                                                val1[:, ds(t, 1)], ALU.is_equal, ALU.mult)
                        nc.vector.tensor_scalar(sort_lo[:, k % 2, 1, :], iota_h[:, 0:P], lo_c[:, ds(t, 1)],
                                                val2[:, ds(t, 1)], ALU.is_equal, ALU.mult)
                        nc.vector.tensor_scalar(sort_hi[:, k % 2, :], iota_h[:, :], hi_c[:, ds(t, 1)], None,
                                                ALU.is_equal).then_inc(sort_ready, 1)
                        low = v.value_load(lo_tab[0:1, ds(t, 1)], min_val=0, max_val=NB - 1)
                        high = v.value_load(hi_tab[0:1, ds(t, 1)], min_val=0, max_val=NB - 1)
                        with v.If(high > low):
                            step = v.value_load(step_tab[0:1, ds(t, 1)], min_val=0, max_val=(ET + 1) * NB)
                            v.wait_ge(acc_done, t + 2)
                            with v.Fori(low + 1, high + 1) as bucket:
                                v.wait_ge(more_acc_done, step + bucket)
                                nc.vector.tensor_scalar(more_rel[:, :], dst_f[:, ds(t, 1)], base[:, ds(bucket, 1)], None,
                                                        ALU.subtract).then_inc(more_rel_set, 1)
                                v.wait_ge(more_rel_set, step + bucket)
                                nc.vector.tensor_scalar(more_hot[:, :], iota[:, 0:P], more_rel[:, :], None,
                                                        ALU.is_equal).then_inc(more_hot_ready, 1)
                                v.wait_ge(more_sum_done, step + bucket)
                                nc.vector.tensor_tensor(acc[:, ds(bucket, 1), 0:D], acc[:, ds(bucket, 1), 0:D],
                                                        ps_more[:, 0:D].unsqueeze(1), ALU.add).then_inc(more_acc_done, 1)
                            v.wait_ge(more_acc_done, step + high + 1)
                            v.nop(nofuse=True)
                        v.wait_ge(sum_done, GROUP + t + 1)
                        v.wait_ge(acc_done, t + 2)
                        nc.vector.tensor_tensor(acc[:, ds(low, 1), 0:D], acc[:, ds(low, 1), 0:D],
                                                ps_sum[k % 2][:, 0:D].unsqueeze(1), ALU.add).then_inc(acc_done, 1)

                v.wait_ge(sort_done, 1)
                nc.vector.tensor_copy(v1_i[:, :], ps_sort[0][:, 0:ST]).then_inc(dec, 1)
                v.wait_ge(dec, 1)
                nc.vector.tensor_scalar(v1_t[:, :], v1_i[:, :], 255, None, ALU.bitwise_and)
                nc.vector.tensor_scalar(v1_i[:, :], v1_i[:, :], 8, None, ALU.arith_shift_right).then_inc(dec, 1)
                v.wait_ge(dec, 2)
                nc.vector.tensor_copy(src_s[:, 0:ST], v1_t[:, :])
                nc.vector.memset(src_s[:, ST:ST + GROUP], 0.0)
                nc.vector.tensor_copy(v1_f[:, :], v1_i[:, :]).then_inc(dec, 1)
                v.wait_ge(dec, 3)
                nc.vector.scalar_tensor_tensor(out=dst_s[:, :], in0=v1_f[:, :], scalar=2048.0, in1=ps_sort[1][:, 0:ST],
                                               op0=ALU.mult, op1=ALU.add)

            @block.tensor
            def _(pe):
                pe.sem_inc(sum_done, GROUP)
                pe.sem_inc(more_sum_done, NB)
                pe.sem_inc(sort_used, 2)
                halves = [(0, 512), (512, ST)]

                def sort(lo, hi, start, stop):
                    for n in range(2):
                        for c, e in halves:
                            last = nc.tensor.matmul(ps_sort[n][:, c:e], lo[n], hi(c, e), start=start, stop=stop)
                    return last

                pe.wait_ge(zero_set, 1)
                zeros = [zero_h[:, 0:P]] * 2
                sort(zeros, lambda c, e: zero_h[:, 0:e - c], True, False)
                with pe.Fori(0, ET // GROUP) as i:
                    for k in range(GROUP):
                        t = i * GROUP + k
                        pe.wait_ge(rows_in[k], (i + 1) * 16)
                        more = pe.value_load(more_tab[0:1, ds(t, 1)], min_val=0, max_val=NB - 1)
                        with pe.If(more > 0):
                            past = pe.value_load(past_tab[0:1, ds(t, 1)], min_val=0, max_val=ET * NB)
                            with pe.Fori(0, more) as m:
                                pe.wait_ge(more_hot_ready, past + m + NB + 1)
                                nc.tensor.matmul(ps_more[:, 0:D], more_hot[:, :], rows[:, k, :],
                                                 start=True, stop=True).then_inc(more_sum_done, 1)
                        pe.wait_ge(hot_ready, t + 1)
                        pe.wait_ge(acc_done, t + 1)
                        nc.tensor.matmul(ps_sum[k % 2][:, 0:D], hot[:, k % 4, :], rows[:, k, :],
                                         start=True, stop=True).then_inc(sum_done, 1)
                        pe.wait_ge(sort_ready, t + 1)
                        sort([sort_lo[:, k % 2, n, :] for n in range(2)],
                             lambda c, e: sort_hi[:, k % 2, c:e], False, False).then_inc(sort_used, 1)
                sort(zeros, lambda c, e: zero_h[:, 0:e - c], False, True).then_inc(sort_done, 1)

        q = sb("q", [P, NT, D])
        with ExitStack() as c3, nc.Block() as block:
            def sb3(name, shape, dt=F32):
                return c3.enter_context(nc.sbuf_tensor(name, shape, dt))

            def ps3(name, shape):
                return c3.enter_context(nc.psum_tensor(name, shape, F32))

            a = sb3("a", [P, 2, D])
            aT = sb3("aT", [D, 2, P])
            h2 = sb3("h2", [P, 2, D])
            hT = sb3("hT", [D, 2, P])
            kv = sb3("kv", [P, 2, 2 * D])
            ps_t = [ps3(f"ps_t{k}", [P, 512]) for k in range(2)]
            ps_w = [ps3(f"ps_w{k}", [P, 512]) for k in range(2)]
            ps_ht = [ps3(f"ps_ht{k}", [P, 512]) for k in range(2)]
            ps_qkv = [ps3(f"ps_qkv{k}", [P, 512]) for k in range(2)]
            a_ready, a_turned, aT_ready, w_done, x1_done, agg = (
                sem("a_ready"), sem("a_turned"), sem("aT_ready"), sem("w_done"), sem("x1_done"), sem("agg"))
            var_ready, std_done, recip_done, norm_ready = sem("var_ready2"), sem("std_done2"), sem("recip_done2"), sem("norm_ready2")
            h2_ready, h2_turned, h2_kept, hT_ready, qkv_done, q_done, kv_ready = (
                sem("h2_ready"), sem("h2_turned"), sem("h2_kept"), sem("hT_ready"), sem("qkv_done"), sem("q_done"), sem("kv_ready"))
            kv_stored = [sem(f"kv_stored{k}") for k in range(2)]
            acc_zero = sem("acc_zero")

            @block.scalar
            def _(act):
                act.sem_inc(q_done, 2)
                with act.Fori(0, NT // 2) as i:
                    for k in range(2):
                        j = i * 2 + k
                        act.wait_ge(a_turned, j + 1)
                        nc.scalar.activation(a[:, k, :], acc[:, ds(j, 1), 0:D], ACT.Copy,
                                             scale=dinv[:, ds(j, 1)]).then_inc(a_ready, 1)
                act.wait_ge(var_ready, 1)
                nc.scalar.activation(rstd[:, :], rstd[:, :], ACT.Sqrt).then_inc(std_done, 1)
                act.wait_ge(norm_ready, 1)

                def normal(j, k):
                    act.wait_ge(h2_turned, j + 1)
                    act.wait_ge(h2_kept, j + 1)
                    nc.scalar.activation(h2[:, k, :], x[:, ds(j, 1), :], ACT.Relu, bias=nbias[:, ds(j, 1)],
                                         scale=rstd[:, ds(j, 1)]).then_inc(h2_ready, 1)

                def keep_q(j, k):
                    act.wait_ge(qkv_done, j + 1)
                    nc.scalar.activation(q[:, ds(j, 1), :], ps_qkv[k][:, 0:D], ACT.Copy).then_inc(q_done, 1)

                normal(0, 0)
                with act.Fori(0, NT // 2 - 1) as i:
                    for k in range(2):
                        normal(i * 2 + k + 1, (k + 1) % 2)
                        keep_q(i * 2 + k, k)
                normal(NT - 1, 1)
                keep_q(NT - 2, 0)
                keep_q(NT - 1, 1)

            @block.tensor
            def _(pe):
                pe.sem_inc(a_turned, 2)
                pe.sem_inc(h2_turned, 2)
                with pe.Fori(0, NT // 2) as i:
                    for k in range(2):
                        j = i * 2 + k
                        pe.wait_ge(a_ready, j + 1)
                        pe.wait_ge(aT_ready, j + 1)
                        nc.tensor.transpose(ps_t[k][:, 0:P], a[:, k, :], ident[:, :]).then_inc(a_turned, 1)
                        pe.wait_ge(aT_ready, j + 3)
                        pe.wait_ge(x1_done, j + 1)
                        nc.tensor.matmul(ps_w[k][:, 0:D], aT[:, k, :], w0[:, :], start=True, stop=False)
                        nc.tensor.matmul(ps_w[k][:, 0:D], ones[0:1, :], b0[:, :], start=False, stop=True).then_inc(w_done, 1)
                with pe.Fori(0, NT // 2) as i:
                    for k in range(2):
                        j = i * 2 + k
                        pe.wait_ge(h2_ready, j + 1)
                        pe.wait_ge(hT_ready, j + 1)
                        nc.tensor.transpose(ps_ht[k][:, 0:P], h2[:, k, :], ident[:, :]).then_inc(h2_turned, 1)
                        pe.wait_ge(hT_ready, j + 3)
                        pe.wait_ge(q_done, j + 1)
                        pe.wait_ge(kv_ready, j + 1)
                        nc.tensor.matmul(ps_qkv[k][:, 0:3 * D], hT[:, k, :], wqkv[:, :], start=True, stop=False)
                        nc.tensor.matmul(ps_qkv[k][:, 0:3 * D], ones[0:1, :], bqkv[:, :],
                                         start=False, stop=True).then_inc(qkv_done, 1)

            @block.gpsimd
            def _(pool):
                pool.sem_inc(h2_kept, 2)
                with pool.Fori(0, NT // 2) as i:
                    for k in range(2):
                        j = i * 2 + k
                        pool.wait_ge(h2_ready, j + 1)
                        nc.gpsimd.tensor_copy(h[:, ds(j, 1), :], h2[:, k, :].unsqueeze(1)).then_inc(h2_kept, 1)

            @block.vector
            def _(v):
                v.sem_inc(aT_ready, 2)
                v.sem_inc(x1_done, 2)
                v.sem_inc(hT_ready, 2)
                v.sem_inc(kv_ready, 2)
                with v.Fori(0, NT // 2) as i:
                    for k in range(2):
                        j = i * 2 + k
                        v.wait_ge(a_turned, j + 3)
                        nc.vector.tensor_copy(aT[:, k, :], ps_t[k][:, 0:P]).then_inc(aT_ready, 1)
                        v.wait_ge(w_done, j + 1)
                        nc.vector.scalar_tensor_tensor(out=x[:, ds(j, 1), :], in0=ps_w[k][:, 0:D].unsqueeze(1), scalar=0.0,
                                                       in1=x[:, ds(j, 1), :], op0=ALU.max, op1=ALU.add).then_inc(x1_done, 1)
                        v.wait_ge(x1_done, j + 3)
                        nc.vector.bn_stats(stats[:, ds(j, 1), :], x[:, ds(j, 1), :]).then_inc(agg, 1)
                steps = [NT]

                def then(ins):
                    steps[0] += 1
                    ins.then_inc(agg, 1)
                    v.wait_ge(agg, steps[0])

                v.wait_ge(agg, NT)
                moments(then, EPS_H).then_inc(var_ready, 1)
                v.wait_ge(std_done, 1)
                nc.vector.reciprocal(rstd[:, :], rstd[:, :]).then_inc(recip_done, 1)
                v.wait_ge(recip_done, 1)
                nc.vector.scalar_tensor_tensor(out=nbias[:, :], in0=mean[:, :], scalar=-1.0, in1=rstd[:, :],
                                               op0=ALU.mult, op1=ALU.mult).then_inc(norm_ready, 1)
                with v.Fori(0, NT // 2) as i:
                    for k in range(2):
                        j = i * 2 + k
                        v.wait_ge(h2_turned, j + 3)
                        nc.vector.tensor_copy(hT[:, k, :], ps_ht[k][:, 0:P]).then_inc(hT_ready, 1)
                        v.wait_ge(q_done, j + 3)
                        v.wait_ge(kv_stored[k], (i + 1) * 16)
                        nc.vector.tensor_copy(kv[:, k, :], ps_qkv[k][:, D:3 * D]).then_inc(kv_ready, 1)
                v.wait_ge(a_ready, NT)
                nc.vector.memset(acc[:, :, :], 0.0).then_inc(acc_zero, 1)

            @block.sync
            def _(sp):
                for k in range(2):
                    sp.sem_inc(kv_stored[k], 16)
                with sp.Fori(0, NT // 2) as i:
                    for k in range(2):
                        j = i * 2 + k
                        sp.wait_ge(kv_ready, j + 3)
                        sp.dma_start(kv_tab[ds(j * P, P), :], kv[:, k, :]).then_inc(kv_stored[k], 16)
                for k in range(2):
                    sp.wait_ge(kv_stored[k], 16 * (NT // 2 + 1))

        QUAD = 4
        with ExitStack() as c4, nc.Block() as block:
            def sb4(name, shape, dt=F32):
                return c4.enter_context(nc.sbuf_tensor(name, shape, dt))

            def ps4(name, shape):
                return c4.enter_context(nc.psum_tensor(name, shape, F32))

            NQ = ST // QUAD
            idx = sb4("idx1", [P, 2, HALF], I32)
            rows = sb4("rows1", [P, GROUP, 2 * D])
            hot = sb4("hot1", [P, 4, QUAD, P])
            hotT = sb4("hotT", [P, 2, QUAD, P])
            prod = sb4("prod", [P, 2, QUAD, D])
            att = sb4("att", [P, 2, QUAD * HEADS])
            attc = sb4("attc", [P, 2, QUAD * HEADS])
            msg = sb4("msg", [P, 2, QUAD, MSG])
            ps_hT = [ps4(f"ps_hT{k}", [P, QUAD, P]) for k in range(2)]
            ps_q = [ps4(f"ps_q{k}", [P, QUAD, D]) for k in range(2)]
            ps_m = [ps4(f"ps_m{k}", [P, 2, 256]) for k in range(4)]
            idx_set, rows_in = sem("idx_set1"), [sem(f"rows_in1_{k}") for k in range(GROUP)]
            hot_ready, turned, hotT_ready, q_ready = sem("hot_ready1"), sem("turned"), sem("hotT_ready"), sem("q_ready")
            prod_done, att_done, clip_done, w_ready, msg_ready, sum_done, acc_done = (
                sem("prod_done"), sem("att_done"), sem("clip_done"), sem("w_ready"), sem("msg_ready"), sem("sum_done1"), sem("acc_done1"))

            @block.gpsimd
            def _(pool):
                with pool.Fori(0, ST // GROUP) as i:
                    for s in range(2):
                        pool.wait_ge(msg_ready, i * QUAD + (s + 1) * 2)
                        nc.gpsimd.tensor_copy(idx[:, s, :], dst_s[:, ds(i * GROUP + s * HALF, HALF)]).then_inc(idx_set, 1)
                        pool.wait_ge(idx_set, i * 2 + s + 1)
                        pool.nop(nofuse=True)
                        for k in range(s * HALF, (s + 1) * HALF):
                            pool.indirect_dma_start(
                                out=rows[:, k, :], out_offset=None, in_=kv_tab,
                                in_offset=bass.IndirectOffsetOnAxis(ap=idx[:, s, k - s * HALF:k - s * HALF + 1], axis=0),
                            ).then_inc(rows_in[k], 16)

            @block.vector
            def _(v):
                v.sem_inc(msg_ready, GROUP // QUAD)
                v.sem_inc(prod_done, 2)
                v.sem_inc(acc_done, 8)

                def one_hot(n, slot):
                    v.wait_ge(sum_done, 2 * n + 2)
                    nc.vector.tensor_tensor(hot[:, slot, :, :],
                                            iota[:, 1:P + 1].unsqueeze(1).to_broadcast([P, QUAD, P]),
                                            src_s[:, ds(n * QUAD, QUAD)].unsqueeze(2).to_broadcast([P, QUAD, P]),
                                            ALU.is_equal).then_inc(hot_ready, 1)

                def scores(i, n, u):
                    s = u % 2
                    v.wait_ge(q_ready, n + 3)
                    for k in range(QUAD):
                        v.wait_ge(rows_in[u * QUAD + k], (i + 1) * 16)
                    nc.vector.tensor_tensor(prod[:, s, :, :], ps_q[s][:, :, :], rows[:, u * QUAD:(u + 1) * QUAD, 0:D],
                                            ALU.mult).then_inc(prod_done, 1)
                    v.wait_ge(prod_done, n + 3)
                    nc.vector.tensor_reduce(att[:, s, :], prod[:, s, :, :].rearrange("p t (h c) -> p (t h) c", c=HD),
                                            AX.X, ALU.add).then_inc(att_done, 1)
                    v.wait_ge(att_done, n + 1)
                    nc.vector.tensor_scalar(attc[:, s, :], att[:, s, :], -40.0, 40.0, ALU.max, ALU.min).then_inc(clip_done, 1)

                def values(n, u):
                    s = u % 2
                    v.wait_ge(w_ready, n + 1)
                    nc.vector.tensor_tensor(
                        msg[:, s, :, 0:D].rearrange("p t (h c) -> p t h c", c=HD),
                        rows[:, u * QUAD:(u + 1) * QUAD, D:2 * D].rearrange("p t (h c) -> p t h c", c=HD),
                        msg[:, s, :, D:MSG].unsqueeze(3).to_broadcast([P, QUAD, HEADS, HD]),
                        ALU.mult).then_inc(msg_ready, 1)

                def sums(n, u):
                    for k in range(QUAD):
                        t = n * QUAD + k
                        b = v.value_load(bucket_tab[0:1, ds(t, 1)], min_val=0, max_val=NB - 1)
                        if k % 2 == 0:
                            v.wait_ge(sum_done, 2 * n + k // 2 + 9)
                        v.wait_ge(acc_done, t + 8)
                        nc.vector.tensor_tensor(acc[:, ds(b, 1), :], acc[:, ds(b, 1), :],
                                                ps_m[2 * (u % 2) + k // 2][:, k % 2:k % 2 + 1, 0:MSG],
                                                ALU.add).then_inc(acc_done, 1)

                def quad(i, u, begun=True):
                    n = i * (GROUP // QUAD) + u
                    one_hot(n + 2, (u + 2) % 4)
                    scores(i, n, u)
                    if begun:
                        sums(n - 1, (u - 1) % 4)
                    values(n, u)

                one_hot(0, 0)
                one_hot(1, 1)
                for u in range(GROUP // QUAD):
                    quad(0, u, u > 0)
                with v.Fori(1, ST // GROUP) as i:
                    for u in range(GROUP // QUAD):
                        quad(i, u)
                sums(NQ - 1, 3)

            @block.scalar
            def _(act):
                act.sem_inc(hotT_ready, 2)

                def copy_turned(n, s):
                    act.wait_ge(turned, n + 1)
                    act.wait_ge(q_ready, n + 1)
                    nc.scalar.activation(hotT[:, s, :, :], ps_hT[s][:, :, :], ACT.Copy).then_inc(hotT_ready, 1)

                copy_turned(0, 0)
                with act.Fori(0, ST // GROUP) as i:
                    for u in range(GROUP // QUAD):
                        n = i * (GROUP // QUAD) + u
                        s = u % 2
                        copy_turned(n + 1, (u + 1) % 2)
                        act.wait_ge(clip_done, n + 1)
                        act.wait_ge(sum_done, 2 * n + 6)
                        nc.scalar.activation(msg[:, s, :, D:MSG], attc[:, s, :].rearrange("p (t h) -> p t h", h=HEADS),
                                             ACT.Exp, scale=0.25).then_inc(w_ready, 1)

            @block.tensor
            def _(pe):
                pe.sem_inc(sum_done, 8)
                pe.sem_inc(q_ready, 2)

                def expand(n, u):
                    s = u % 2
                    pe.wait_ge(hot_ready, n + 1)
                    pe.wait_ge(hotT_ready, n + 1)
                    for k in range(QUAD):
                        last = nc.tensor.transpose(ps_hT[s][:, k, :], hot[:, u % 4, k, :], ident[:, :])
                    last.then_inc(turned, 1)
                    pe.wait_ge(hotT_ready, n + 3)
                    pe.wait_ge(prod_done, n + 1)
                    for k in range(QUAD):
                        b = pe.value_load(bucket_tab[0:1, ds(n * QUAD + k, 1)], min_val=0, max_val=NB - 1)
                        last = nc.tensor.matmul(ps_q[s][:, k, :], hotT[:, s, k, :], q[:, ds(b, 1), :], start=True, stop=True)
                    last.then_inc(q_ready, 1)

                expand(0, 0)
                with pe.Fori(0, ST // GROUP) as i:
                    for u in range(GROUP // QUAD):
                        n = i * (GROUP // QUAD) + u
                        expand(n + 1, (u + 1) % 4)
                        pe.wait_ge(msg_ready, n + 5)
                        for g in range(2):
                            pe.wait_ge(acc_done, n * QUAD + 2 * g + 2)
                            for k in (2 * g, 2 * g + 1):
                                last = nc.tensor.matmul(ps_m[2 * (u % 2) + g][:, k % 2, 0:MSG], hot[:, u, k, :],
                                                        msg[:, u % 2, k, :], start=True, stop=True)
                            last.then_inc(sum_done, 1)

        with ExitStack() as c5, nc.Block() as block:
            den = c5.enter_context(nc.sbuf_tensor("den", [P, NT, HEADS], F32))
            step, var_ready, std_done, norm_ready, normed, out_ready, stored = (
                sem("step5"), sem("var_ready3"), sem("std_done3"), sem("norm_ready3"), sem("normed"), sem("out_ready"), sem("stored"))

            @block.vector
            def _(v):
                steps = [0]

                def then(ins):
                    steps[0] += 1
                    ins.then_inc(step, 1)
                    v.wait_ge(step, steps[0])

                then(nc.vector.tensor_scalar(den[:, :, :], acc[:, :, D:MSG], EPS_SUM, None, ALU.add))
                then(nc.vector.reciprocal(den[:, :, :], den[:, :, :]))
                then(nc.vector.tensor_tensor(acc[:, :, 0:D].rearrange("p j (h c) -> p j h c", c=HD),
                                             acc[:, :, 0:D].rearrange("p j (h c) -> p j h c", c=HD),
                                             den[:, :, :].unsqueeze(3).to_broadcast([P, NT, HEADS, HD]), ALU.mult))
                then(nc.vector.tensor_tensor(h[:, :, :], h[:, :, :], acc[:, :, 0:D], ALU.add))
                with v.Fori(0, NT) as j:
                    nc.vector.bn_stats(stats[:, ds(j, 1), :], h[:, ds(j, 1), :]).then_inc(step, 1)
                steps[0] += NT
                v.wait_ge(step, steps[0])
                moments(then, EPS_OUT).then_inc(var_ready, 1)
                v.wait_ge(std_done, 1)
                then(nc.vector.reciprocal(rstd[:, :], rstd[:, :]))
                nc.vector.scalar_tensor_tensor(out=nbias[:, :], in0=mean[:, :], scalar=-1.0, in1=rstd[:, :],
                                               op0=ALU.mult, op1=ALU.mult).then_inc(norm_ready, 1)
                v.wait_ge(normed, NT)
                then(nc.vector.tensor_tensor(h[:, :, :], h[:, :, :], gamma[:, :].unsqueeze(1).to_broadcast([P, NT, D]), ALU.mult))
                then(nc.vector.tensor_tensor(x[:, :, :], x[:, :, :], beta[:, :].unsqueeze(1).to_broadcast([P, NT, D]), ALU.add))
                nc.vector.tensor_tensor(h[:, :, :], h[:, :, :], x[:, :, :], ALU.add).then_inc(out_ready, 1)

            @block.scalar
            def _(act):
                act.wait_ge(var_ready, 1)
                nc.scalar.activation(rstd[:, :], rstd[:, :], ACT.Sqrt).then_inc(std_done, 1)
                act.wait_ge(norm_ready, 1)
                with act.Fori(0, NT) as j:
                    nc.scalar.activation(h[:, ds(j, 1), :], h[:, ds(j, 1), :], ACT.Identity, bias=nbias[:, ds(j, 1)],
                                         scale=rstd[:, ds(j, 1)]).then_inc(normed, 1)

            @block.sync
            def _(sp):
                sp.wait_ge(out_ready, 1)
                sp.dma_start(out, h[:, :, :]).then_inc(stored, 16)
                sp.wait_ge(stored, 16)


def kernel(**inputs):
    import numpy as np
    import concourse.bacc as bacc
    from concourse.bass_utils import run_bass_kernel_spmd as run

    def lanes(a, count):
        a = np.concatenate([a, np.repeat(a[-1:], count * P - len(a), axis=0)])
        return np.ascontiguousarray(np.swapaxes(a.reshape(count, P, *a.shape[1:]), 0, 1))

    given = {k: np.asarray(v) for k, v in inputs.items()}
    wide = lambda a: np.ascontiguousarray(np.broadcast_to(a, (P, len(a))))
    dst_rows = lanes(given["dst"], 7 * P)
    arrays = {
        "x_in": lanes(given["x"], NT),
        "src_in": lanes(given["src"], ET),
        "dst_in": lanes(given["dst"], ET),
        "dst_rows_in": np.ascontiguousarray(dst_rows.T.reshape(7, P, P).swapaxes(0, 1)),
        "w0_in": np.ascontiguousarray(given["L0_gnn_W"]),
        "b0_in": given["L0_gnn_b"].reshape(1, D),
        "wqkv_in": np.ascontiguousarray(np.concatenate([given[f"L1_gnn_W{n}"].T for n in "qkv"], axis=1)),
        "bqkv_in": np.concatenate([given[f"L1_gnn_b{n}"] for n in "qkv"]).reshape(1, 3 * D),
        "gamma_in": wide(given["L1_gnn_gamma"]),
        "beta_in": wide(given["L1_gnn_beta"]),
    }
    nc = bacc.Bacc("TRN2", target_bir_lowering=False, num_devices=1)
    args = {n: nc.dram_tensor(n, a.shape, mybir.dt.from_np(a.dtype), kind="ExternalInput").ap() for n, a in arrays.items()}
    args["y_tab"] = nc.dram_tensor("y_tab", (NT * P, D), F32, kind="Internal").ap()
    args["kv_tab"] = nc.dram_tensor("kv_tab", (NT * P, 2 * D), F32, kind="Internal").ap()
    args["out"] = nc.dram_tensor("out", (P, NT, D), F32, kind="ExternalOutput").ap()
    build(nc, **args)
    result = run(nc, [arrays], core_ids=[0]).results[0]["out"]
    return np.ascontiguousarray(np.swapaxes(result, 0, 1).reshape(NT * P, D)[:NODES])
```
